# Optimizing a Trainium2 kernel written in Bass

```python
import numpy as np
import jax
import jax.numpy as jnp

def _softmax(x, axis=-1):
    return jax.nn.softmax(x, axis=axis)

def _gelu(x):
    return jax.nn.gelu(x, approximate=True)

def _silu(x):
    return jax.nn.silu(x)

def _sigmoid(x):
    return jax.nn.sigmoid(x)

def _layernorm(x, axis=-1, eps=1e-05):
    m = jnp.mean(x, axis=axis, keepdims=True)
    v = jnp.var(x, axis=axis, keepdims=True)
    return (x - m) / jnp.sqrt(v + eps)

def _scatter_add(tgt, idx, src, axis=0):
    return tgt.at[idx].add(src)

def _segment_sum(src, seg, n):
    return jax.ops.segment_sum(src, seg, n)
kernel_name = 'mk_flamingo_gated_d1_seqx_r4_9af99c'

def setup_inputs(seed: int=0):
    np.random.seed(seed)
    _w = jnp.asarray

    def _rec_inputs():
        import jax
        import jax.numpy as jnp
        _rk = jax.random.key(seed)
        x = -0.0003929 + 0.9999 * jax.random.normal(jax.random.fold_in(_rk, 1), (8, 256, 256), jnp.float32)
        _lenS = 256 - jax.random.randint(jax.random.fold_in(_rk, 7), (8,), 0, max(1, 256 // 4) + 1, jnp.int32)
        _lenS2 = 120 - jax.random.randint(jax.random.fold_in(_rk, 8), (8,), 0, max(1, 120 // 4) + 1, jnp.int32)
        _ctx_1024P = jax.random.normal(jax.random.fold_in(_rk, 11), (8, 16, 256), jnp.float32)
        _ctx_1024c = jax.random.dirichlet(jax.random.fold_in(_rk, 511), 0.3 * jnp.ones((16,), jnp.float32), (8, 120))
        _ctx_1024t = jnp.einsum('bsk,bkd->bsd', _ctx_1024c, _ctx_1024P)
        _ctx_1024t = _ctx_1024t * jax.lax.rsqrt(jnp.mean(jnp.square(_ctx_1024t)) + 1e-12) * 0.953939
        ctx_1024 = 2.81802e-05 + 1.00001 * (_ctx_1024t + 0.3 * jax.random.normal(jax.random.fold_in(_rk, 611), (8, 120, 256), jnp.float32))
        _g = jax.random.normal(jax.random.fold_in(_rk, 9001), (2, 1), jnp.float32)
        _g = jnp.sign(_g) * jnp.maximum(jnp.abs(_g), 1.0) + (_g == 0) * 1.0
        g_xattn = _g[0]
        g_ffn = _g[1]
        return (x, ctx_1024, g_xattn, g_ffn)
    x, ctx_1024, g_xattn, g_ffn = _rec_inputs()

    def _L0_xattn_setup():
        import jax, jax.numpy as jnp
        import numpy as np
        QUERY_DIM = 256
        HIDDEN_DIM = 256
        key = jax.random.key(seed)
        k1, k2, k3, k4 = jax.random.split(key, 4)
        query = jax.random.normal(k1, (8, 512, QUERY_DIM), dtype=jnp.float32)
        info = jax.random.normal(k2, (8, 512, HIDDEN_DIM), dtype=jnp.float32)
        bound = 1.0 / np.sqrt(QUERY_DIM)
        W = jax.random.uniform(k3, (HIDDEN_DIM, QUERY_DIM), jnp.float32, -bound, bound)
        b = jax.random.uniform(k4, (HIDDEN_DIM,), jnp.float32, -bound, bound)
        return {'query': query, 'info': info, 'W': W, 'b': b}
    _L0_xattn_all = _L0_xattn_setup()
    _L0_xattn_in = {k: v for k, v in _L0_xattn_all.items() if k in ('W', 'b')}
    del _L0_xattn_all

    def _L0_ffn_setup():
        import jax, jax.numpy as jnp
        import numpy as np
        N_HEADS = 4
        key = jax.random.key(seed)
        k1, k2, k3, k4 = jax.random.split(key, 4)
        dmodel, n_experts, expert_size = (256, 64, 128)
        B, S = (4, 512)
        x = jax.random.normal(k1, (B, S, dmodel), dtype=jnp.float32)
        expert_sel = jax.random.normal(k2, (n_experts, dmodel), dtype=jnp.float32) * dmodel ** (-0.5)
        keys = jax.random.normal(k3, (n_experts, dmodel, expert_size), dtype=jnp.float32) * dmodel ** (-0.5)
        values = jax.random.normal(k4, (n_experts, expert_size, dmodel), dtype=jnp.float32) * (n_experts * expert_size) ** (-0.5)
        return {'x': x, 'expert_sel': expert_sel, 'keys': keys, 'values': values}
    _L0_ffn_all = _L0_ffn_setup()
    _L0_ffn_in = {k: v for k, v in _L0_ffn_all.items() if k in ('expert_sel', 'keys', 'values')}
    del _L0_ffn_all
    return {'x': x, 'ctx_1024': ctx_1024, 'g_xattn': g_xattn, 'g_ffn': g_ffn, 'L0_xattn_W': _L0_xattn_in['W'], 'L0_xattn_b': _L0_xattn_in['b'], 'L0_ffn_expert_sel': _L0_ffn_in['expert_sel'], 'L0_ffn_keys': _L0_ffn_in['keys'], 'L0_ffn_values': _L0_ffn_in['values']}

def reference(x, ctx_1024, g_xattn, g_ffn, L0_xattn_W, L0_xattn_b, L0_ffn_expert_sel, L0_ffn_keys, L0_ffn_values):
    import jax
    import jax.numpy as jnp

    def _L0_xattn_ref(query, info, W, b):
        import jax, jax.numpy as jnp
        import numpy as np
        QUERY_DIM = 256
        HIDDEN_DIM = 256
        q = jnp.einsum('bsq,hq->bsh', query, W) + b
        scores = jax.nn.softmax(jnp.einsum('bsh,bmh->bsm', q, info), axis=-1)
        return jnp.einsum('bsm,bmh->bsh', scores, info)

    def _L0_ffn_ref(x, expert_sel, keys, values):
        import jax, jax.numpy as jnp
        import numpy as np
        N_HEADS = 4
        B, S, d = x.shape
        n_experts = keys.shape[0]
        xf = x.reshape(-1, d)
        N = xf.shape[0]
        logits = xf @ expert_sel.T
        sel = jax.nn.sigmoid(logits)
        sel_val, sel_idx = jax.lax.top_k(sel, N_HEADS)
        gates = jnp.zeros((N, n_experts), dtype=x.dtype)
        gates = gates.at[jnp.arange(N)[:, None], sel_idx].set(sel_val)
        h = jnp.einsum('nd,kde->nke', xf, keys)
        scores = jax.nn.relu(h) * gates[:, :, None]
        out = jnp.einsum('nke,kev->nv', scores, values)
        return out.reshape(B, S, -1)
    x = x + jnp.tanh(g_xattn[0]) * _L0_xattn_ref(_layernorm(x, axis=-1), ctx_1024, L0_xattn_W, L0_xattn_b)
    x = x + jnp.tanh(g_ffn[0]) * _L0_ffn_ref(_layernorm(x, axis=-1), L0_ffn_expert_sel, L0_ffn_keys, L0_ffn_values)
    return x

_drawn_inputs = setup_inputs


def setup_inputs(seed=0):
    import zlib

    import numpy as np

    out = dict(_drawn_inputs(seed))
    spreads = {}
    factors = {}
    for name, (base, spread) in spreads.items():
        noise = np.random.default_rng([zlib.crc32(name.encode()), seed]).standard_normal(out[name].shape)
        drawn = base * np.exp(spread * noise) if base else spread * noise
        out[name] = jnp.asarray(drawn.astype(out[name].dtype))
    for name, factor in factors.items():
        out[name] = (out[name] * factor).astype(out[name].dtype)
    return out
```

```python
from contextlib import ExitStack

import concourse.bass as bass
from concourse import mybir
from concourse.bass import ds

F32 = mybir.dt.float32
BF16 = mybir.dt.bfloat16
F16 = mybir.dt.float16
I32 = mybir.dt.int32
U32 = mybir.dt.uint32
ALU = mybir.AluOpType
ACT = mybir.ActivationFunctionType
AX = mybir.AxisListType

P = 128
EPS = 1e-5


class At:

    def __init__(self, offset, register=None, step=0):
        self.offset, self.register, self.step = offset, register, step

    def __add__(self, n):
        return At(self.offset + n, self.register, self.step)

    def __sub__(self, n):
        return self + -n

    @property
    def value(self):
        return self.offset if self.register is None else self.register * self.step + self.offset

    def div(self, n):
        return At(self.offset // n, self.register, self.step // n)

    def mod(self, n):
        return self.offset % n


def row(ap, at):
    return ap[:, ds(at.value, 1), :].rearrange("p a n -> p (a n)")


def after(engine, semaphore, count, each=1):
    if count.register is None and count.offset <= 0:
        return
    engine.wait_ge(semaphore, count.value * each)


def flamingo_block(nc, x, ctx, g_xattn, g_ffn, w_q, b_q, expert_sel, keys, values, out):
    B, S, D = x.shape
    M = ctx.shape[1]
    E = expert_sel.shape[0]
    F = keys.shape[2]
    K = 4
    N = B * S
    C = D // P
    T = N // P
    TB = S // P
    U = 4
    LEAD = 3
    NT = -(-(E + (N * K - E) // P) // U) * U
    TURNS = NT // U
    FULL = N * K // P // U
    NX = NT + LEAD
    HALF = B // 2 * M
    XCH = 4
    assert (D, M <= P, F, C, TB, E <= P, NT <= P) == (2 * P, True, P, 2, 2, True, True)

    x_tiles = x.rearrange("b (s p) d -> p (b s) d", p=P)
    out_tiles = out.rearrange("b (s p) d -> p (b s) d", p=P)
    xn_rows = nc.dram_tensor("xn_rows", [N, D], F32).ap()
    xn_tiles = xn_rows.rearrange("(t p) d -> p t d", p=P)
    y_rows = nc.dram_tensor("y_rows", [NT * P, D], F32).ap()
    y_tiles = y_rows.rearrange("(t p) d -> p t d", p=P)

    with ExitStack() as stack:
        def sb(name, shape, dt=F32):
            return stack.enter_context(nc.sbuf_tensor(name, shape, dt))

        def sem(name):
            return stack.enter_context(nc.semaphore(name))

        bank = stack.enter_context(nc.psum_tensor("bank", [P, 8, 512], F32))

        keys_sb = sb("keys_sb", [P, E * C, F])
        values_sb = sb("values_sb", [P, E, D])
        xs = sb("xs", [P, T, D])
        ctx_sb = sb("ctx_sb", [M, B, D])
        early_a = sb("early_a", [P, C * B * M])
        early_b = sb("early_b", [P, C * B * M])
        ctxT = early_a[:].rearrange("p (c m) -> p c m", c=C)
        wq_sb = sb("wq_sb", [P, C, D])
        bq_rows = sb("bq_rows", [C, P])
        bq_sb = sb("bq_sb", [P, C])
        m_sb = early_b[:].rearrange("p (c m) -> p c m", m=M)
        bias_row = sb("bias_row", [1, B, M])
        sel_sb = sb("sel_sb", [E, D])
        selT = sb("selT", [P, C, E])
        xn = sb("xn", [P, 4, D])
        xnT = sb("xnT", [P, 2, D])
        probs = sb("probs", [P, 2, M])
        probsT = sb("probsT", [M, 2, P])
        stats = sb("stats", [P, T, 2, 3])
        moments = sb("moments", [P, 4, T])
        mean = sb("mean", [P, T])
        var = sb("var", [P, T])
        std = sb("std", [P, T])
        rstd = sb("rstd", [P, T])
        neg_max = sb("neg_max", [P, T])
        row_sum = sb("row_sum", [P, T])
        inv_sum = sb("inv_sum", [P, T])
        gates_in = sb("gates_in", [P, 2])
        gate_tanh = sb("gate_tanh", [P, 2])
        ident = sb("ident", [P, P])
        ones_row = sb("ones_row", [1, P])
        ones_bf = sb("ones_bf", [P, P], BF16)
        before = sb("before", [P, P], BF16)
        upto = sb("upto", [P, P], BF16)
        iota_f = sb("iota_f", [P, P])
        iota_h = sb("iota_h", [P, P], F16)
        token_no = sb("token_no", [P, T])
        probs_sel = sb("probs_sel", [P, 2, E])
        top = sb("top", [P, 4, 8])
        top_at = sb("top_at", [P, 4, 8], U32)
        chosen = sb("chosen", [P, T * K, E], BF16)
        cum = sb("cum", [P, 2, K * E], BF16)
        rank = sb("rank", [P, T, E])
        picked = early_a[:, 0:4 * K * E].rearrange("p (k e) -> p k e", e=E)
        gate = sb("gate", [P, T * K])
        pos_f = sb("pos_f", [P, T * K])
        pos_i = sb("pos_i", [P, T * K], I32)
        part_i = sb("part_i", [P, 2, T * K], I32)
        lane_f = sb("lane_f", [P, T * K])
        tile_f = sb("tile_f", [P, T * K])
        base_sb = sb("base_sb", [P, E])
        count_i = sb("count_i", [E, 2], I32)
        tiles_bf = sb("tiles_bf", [E, P], BF16)
        end_f = sb("end_f", [E, 1])
        done_bf = sb("done_bf", [E, P], BF16)
        expert_of = sb("expert_of", [1, NT + 2 * U], I32)
        total_i = sb("total_i", [1, 1], I32)
        HOT = 4
        lane_hot = sb("lane_hot", [P, HOT, P], F16)
        tile_hot = sb("tile_hot", [P, HOT, P], F16)
        empty_f = sb("empty_f", [P, P])
        slot_token = sb("slot_token", [P, NX + 1], U32)
        xg, xgT = xn, xnT
        y_sb = early_b[:, 0:U * D].rearrange("p (u d) -> p u d", u=U)
        YG = 4
        yg = early_a[:, 0:YG * D].rearrange("p (u d) -> p u d", u=YG)
        hid = early_a[:, YG * D:YG * D + 2 * F].rearrange("p (u d) -> p u d", u=2)
        hidT = early_a[:, YG * D + 2 * F:YG * D + 2 * F + 2 * P].rearrange("p (u d) -> p u d", u=2)

        def pT(i): return bank[:, i, 0:D]
        def pS(i): return bank[:, 2 + i, 0:M]
        def pPT(i): return bank[0:M, 4 + i, 0:P]
        def pO(i): return bank[:, 6 + i, 0:D]
        def pL(i): return bank[:, 2 + i, 0:E]
        def pR(i): return bank[:, 4 + i, 0:E]
        def pH(i): return bank[:, 2 + i, 0:F]
        def pHT(i): return bank[:, 4 + i, 0:P]
        count_ps = bank[0:E, 6, 0:1]
        base_ps = bank[:, 6, 64:64 + E]
        end_ps = bank[0:E, 6, 192:193]
        expert_ps = bank[0:1, 6, 256:256 + P]
        total_ps = bank[0:1, 6, 448:449]
        slot_ps = bank[:, 7, 0:P]

        x_in = [sem(f"x_in{i}") for i in range(XCH)]
        ctx_in, wq_in, bq_in, sel_in, g_in = (sem(f"{n}_in") for n in ("ctx", "wq", "bq", "sel", "g"))
        weights_in = sem("weights_in")
        ident_ok, consts_ok, pool_own = sem("ident_ok"), sem("consts_ok"), sem("pool_own")
        tanh_ok, ctx_scaled = sem("tanh_ok"), sem("ctx_scaled")
        setup_t, setup_t_copied = sem("setup_t"), sem("setup_t_copied")
        setup_m, setup_m_copied = sem("setup_m"), sem("setup_m_copied")
        a_stats, m_own, var_ok, std_ok, rstd_ok = (
            sem(n) for n in ("a_stats", "m_own", "var_ok", "std_ok", "rstd_ok"))
        a_xn, a_T, a_Tc, a_S, a_max, a_exp, a_PT, a_PTc, a_O, a_inv, a_x2 = (
            sem(f"a_{n}") for n in ("xn", "T", "Tc", "S", "max", "exp", "PT", "PTc", "O", "inv", "x2"))
        b_stats, b_xn, b_T, b_Tc, b_L, b_sel, b_top, b_kept, b_at, b_hot, b_cum, b_R, b_rank = (
            sem(f"b_{n}") for n in ("stats", "xn", "T", "Tc", "L", "sel", "top", "kept", "at", "hot", "cum",
                                    "R", "rank"))
        xn_out = [sem(f"xn_out{i}") for i in range(4)]
        r_count, r_own, r_tiles, r_base, r_end, r_done, r_expert, r_experts_ok = (
            sem(f"r_{n}") for n in ("count", "own", "tiles", "base", "end", "done", "expert", "experts_ok"))
        r_hot, r_used, r_slots, r_pos_ok, r_slot_ok = (
            sem(f"r_{n}") for n in ("hot", "used", "slots", "pos_ok", "slot_ok"))
        xg_in = [sem(f"xg_in{i}") for i in range(U)]
        e_T, e_Tc, e_H, e_h, e_HT, e_hT, e_Y, e_y = (
            sem(f"e_{n}") for n in ("T", "Tc", "H", "h", "HT", "hT", "Y", "y"))
        y_filled = sem("y_filled")
        y_out = [sem(f"y_out{i}") for i in range(U)]
        yg_in = [sem(f"yg_in{i}") for i in range(YG)]
        yg_used, out_done = sem("yg_used"), sem("out_done")

        block = stack.enter_context(nc.Block())

        def pipeline(eng, step, last, unroll):
            first = -(-(last + 2) // unroll) * unroll
            for s in range(first):
                step(At(s), s)
            with eng.Fori(first // unroll, T // unroll) as i:
                for u in range(unroll):
                    step(At(u, i, unroll), None)
            for s in range(T, T + last):
                step(At(s), s)

        def all_turns(eng, turn, instead=None):
            used = used_tiles(eng)
            turn(At(0))
            with eng.Fori(1, FULL) as i:
                turn(At(0, i, U))
            with eng.Fori(FULL, TURNS) as i:
                with eng.If(used > i * U):
                    turn(At(0, i, U))
                if instead:
                    with eng.Else():
                        instead()

        def used_tiles(eng):
            eng.wait_ge(r_experts_ok, 2)
            return nc.values_load_multi_w_load_instructions(
                total_i[0:1, 0:1], engines=[eng.engine], min_val=N * K // P, max_val=NT,
                skip_runtime_bounds_check_because="it is a sum over experts of ceil(count / P)")[1][0]

        def live(at, s, behind):
            return s is None or 0 <= s - behind < T

        @block.sync
        def _(sp):
            per = T // XCH
            sp.dma_start(xs[:, 0:per, :], x_tiles[:, 0:per, :]).then_inc(x_in[0], 16)
            sp.dma_start(ctx_sb[:], ctx.rearrange("b m d -> m b d")).then_inc(ctx_in, 16)
            sp.dma_start(wq_sb[:], w_q.rearrange("(c p) q -> p c q", p=P)).then_inc(wq_in, 16)
            for n in range(1, XCH):
                sp.dma_start(xs[:, n * per:(n + 1) * per, :],
                             x_tiles[:, n * per:(n + 1) * per, :]).then_inc(x_in[n], 16)
            k_src = keys.rearrange("e (c p) f -> p (e c) f", p=P)
            v_src = values.rearrange("e f d -> f e d")
            for n in range(0, E, 8):
                sp.dma_start(keys_sb[:, n * C:(n + 8) * C, :],
                             k_src[:, n * C:(n + 8) * C, :]).then_inc(weights_in, 16)
                sp.dma_start(values_sb[:, n:n + 8, :], v_src[:, n:n + 8, :]).then_inc(weights_in, 16)

            def store_xn(t):
                after(sp, b_xn, t + 1)
                sp.dma_start(xn_tiles[:, ds(t.value, 1), :], xn[:, t.mod(4):t.mod(4) + 1, :]
                             ).then_inc(xn_out[t.mod(4)], 16)

            with sp.Fori(0, T // 4) as i:
                for u in range(4):
                    store_xn(At(u, i, 4))

            def store_results(t):
                for u in range(U):
                    after(sp, e_y, t + u + 1)
                    sp.dma_start(y_tiles[:, ds((t + u).value, 1), :], y_sb[:, u:u + 1, :]
                                 ).then_inc(y_out[u], 16)

            def no_results():
                for u in range(U):
                    sp.sem_inc(y_out[u], 16)

            sp.wait_ge(y_filled, 16)
            all_turns(sp, store_results, no_results)

            with sp.Fori(0, T) as i:
                t = At(0, i, 1)
                after(sp, yg_used, t + 1, K)
                sp.dma_start(out_tiles[:, ds(t.value, 1), :], xs[:, ds(t.value, 1), :]
                             ).then_inc(out_done, 16)
            sp.wait_ge(out_done, 16 * T)

        @block.gpsimd
        def _(pool):
            pool.memset(ident[:], 0.0).then_inc(pool_own, 1)
            pool.wait_ge(pool_own, 1)
            pool.affine_select(out=ident[:], in_=ident[:], compare_op=ALU.not_equal, fill=1.0, base=0,
                               pattern=[[-1, P]], channel_multiplier=1).then_inc(ident_ok, 1)
            pool.memset(ones_row[:], 1.0).then_inc(consts_ok, 1)
            pool.memset(ones_bf[:], 1.0).then_inc(consts_ok, 1)
            pool.wait_ge(consts_ok, 2)
            pool.affine_select(out=before[:], in_=ones_bf[:], compare_op=ALU.is_gt, fill=0.0, base=0,
                               pattern=[[1, P]], channel_multiplier=-1).then_inc(consts_ok, 1)
            pool.affine_select(out=upto[:], in_=ones_bf[:], compare_op=ALU.is_ge, fill=0.0, base=0,
                               pattern=[[1, P]], channel_multiplier=-1).then_inc(consts_ok, 1)
            pool.iota(iota_f[:], pattern=[[1, P]], base=0, channel_multiplier=0,
                      allow_small_or_imprecise_dtypes=True).then_inc(consts_ok, 1)
            pool.iota(iota_h[:], pattern=[[1, P]], base=0, channel_multiplier=0,
                      allow_small_or_imprecise_dtypes=True).then_inc(consts_ok, 1)
            pool.iota(token_no[:], pattern=[[P, T]], base=1, channel_multiplier=1,
                      allow_small_or_imprecise_dtypes=True).then_inc(consts_ok, 1)
            pool.memset(cum[:, 0, :], 0.0).then_inc(consts_ok, 1)

            def add_up(t):
                after(pool, b_top, t + 1)
                pool.tensor_copy(gate[:, ds(t.value * K, K)], top[:, t.mod(4), 0:K]).then_inc(b_kept, 1)
                after(pool, b_hot, t + 1)
                after(pool, b_R, t)
                after(pool, b_cum, t)
                pool.tensor_tensor(
                    cum[:, (t.offset + 1) % 2, :], cum[:, t.mod(2), :],
                    chosen[:, ds(t.value * K, K), :].rearrange("p k e -> p (k e)"),
                    ALU.add).then_inc(b_cum, 1)

            pool.wait_ge(consts_ok, 8)
            for u in range(4):
                add_up(At(u))
            with pool.Fori(1, T // 4) as i:
                for u in range(4):
                    add_up(At(u, i, 4))

            pool.wait_ge(r_slot_ok, 2)
            for n in range(4):
                pool.wait_ge(xn_out[n], 16 * T // 4)

            used = used_tiles(pool)

            def gather_rows(tiles):
                for t in tiles:
                    if t >= U:
                        pool.wait_ge(e_T, t - U + 1)
                    pool.indirect_dma_start(
                        xg[:, t % U, :], None, xn_rows,
                        bass.IndirectOffsetOnAxis(ap=slot_token[:, t:t + 1], axis=0),
                        bounds_check=N - 1, oob_is_err=False).then_inc(xg_in[t % U], 16)

            gather_rows(range(LEAD + FULL * U))
            for n in range(FULL, TURNS):
                with pool.If(used > n * U):
                    gather_rows(range(LEAD + n * U, LEAD + (n + 1) * U))

            for n in range(U):
                pool.wait_ge(y_out[n], 16 * TURNS)
            for n in range(T * K):
                if n >= YG:
                    pool.wait_ge(yg_used, n - YG + 1)
                pool.indirect_dma_start(
                    yg[:, n % YG, :], None, y_rows, bass.IndirectOffsetOnAxis(ap=pos_i[:, n:n + 1].bitcast(U32), axis=0),
                    bounds_check=NT * P - 1, oob_is_err=False).then_inc(yg_in[n % YG], 16)

        @block.tensor
        def _(pe):
            pe.wait_ge(ident_ok, 1)
            pe.wait_ge(ctx_in, 16)
            for n in range(B // 2):
                for b in (2 * n, 2 * n + 1):
                    for c in range(C):
                        at = ((b % 2) * C + c) * M
                        mm = pe.transpose(bank[:, 2 + n, at:at + M], ctx_sb[:, b, c * P:(c + 1) * P],
                                          ident[0:M, 0:M])
                mm.then_inc(setup_t, 1)
            pe.wait_ge(sel_in, 16)
            for c in range(C):
                mm = pe.transpose(bank[:, 6, c * E:(c + 1) * E], sel_sb[:, c * P:(c + 1) * P],
                                  ident[0:E, 0:E])
            mm.then_inc(setup_t, 1)
            pe.wait_ge(bq_in, 16)
            pe.transpose(bank[:, 7, 0:C], bq_rows[:], ident[0:C, 0:C]).then_inc(setup_t, 1)
            pe.wait_ge(wq_in, 16)
            pe.wait_ge(setup_t_copied, 6)
            banks = [2, 3, 4, 5]
            for n, (cq, half) in enumerate((cq, half) for cq in range(C) for half in range(2)):
                for c in range(C):
                    mm = pe.matmul(bank[:, banks[n], 0:HALF], wq_sb[:, c, cq * P:(cq + 1) * P],
                                   ctxT[:, c, half * HALF:(half + 1) * HALF], start=c == 0, stop=c == C - 1)
                mm.then_inc(setup_m, 1)
            for half in range(2):
                for c in range(C):
                    mm = pe.matmul(bank[0:1, 6 + half, 0:HALF], bq_sb[:, c:c + 1],
                                   ctxT[:, c, half * HALF:(half + 1) * HALF], start=c == 0, stop=c == C - 1)
                mm.then_inc(setup_m, 1)
            pe.wait_ge(setup_m_copied, 6)
            pe.wait_ge(consts_ok, 8)

            def attend(at, s):
                if live(at, s, 0):
                    t = at
                    after(pe, a_xn, t + 1)
                    after(pe, a_Tc, t - 1)
                    for c in range(C):
                        mm = pe.transpose(pT(t.mod(2))[:, c * P:(c + 1) * P],
                                          xn[:, t.mod(2), c * P:(c + 1) * P], ident[:])
                    mm.then_inc(a_T, 1)
                if live(at, s, 1):
                    t = at - 1
                    after(pe, a_Tc, t + 1)
                    after(pe, a_exp, t - 1)
                    for c in range(C):
                        pe.matmul(pS(t.mod(2)), xnT[:, t.mod(2), c * P:(c + 1) * P],
                                  row(m_sb, t.div(TB) + c * B), start=c == 0, stop=False)
                    pe.matmul(pS(t.mod(2)), ones_row[:], row(bias_row, t.div(TB)),
                              start=False, stop=True).then_inc(a_S, 1)
                if live(at, s, 2):
                    t = at - 2
                    after(pe, a_exp, t + 1)
                    after(pe, a_PTc, t - 1)
                    pe.transpose(pPT(t.mod(2)), probs[:, t.mod(2), :], ident[:]).then_inc(a_PT, 1)
                if live(at, s, 3):
                    t = at - 3
                    after(pe, a_PTc, t + 1)
                    after(pe, a_x2, t - 1)
                    pe.matmul(pO(t.mod(2)), probsT[:, t.mod(2), :], row(ctx_sb, t.div(TB)),
                              start=True, stop=True).then_inc(a_O, 1)

            pe.wait_ge(ctx_scaled, 1)
            pipeline(pe, attend, 3, 2)

            def route(at, s):
                if live(at, s, 0):
                    t = at
                    after(pe, b_xn, t + 1)
                    after(pe, b_Tc, t - 1)
                    for c in range(C):
                        mm = pe.transpose(pT(t.mod(2))[:, c * P:(c + 1) * P],
                                          xn[:, t.mod(4), c * P:(c + 1) * P], ident[:])
                    mm.then_inc(b_T, 1)
                if live(at, s, 1):
                    t = at - 1
                    after(pe, b_Tc, t + 1)
                    after(pe, b_sel, t - 1)
                    for c in range(C):
                        mm = pe.matmul(pL(t.mod(2)), xnT[:, t.mod(2), c * P:(c + 1) * P],
                                       selT[:, c, :], start=c == 0, stop=c == C - 1)
                    mm.then_inc(b_L, 1)
                if live(at, s, 4):
                    t = at - 4
                    after(pe, b_hot, t + 1)
                    after(pe, b_cum, t)
                    after(pe, b_rank, t - 1)
                    for k in range(K):
                        pe.matmul(pR(t.mod(2)), before[:], row(chosen, At(t.offset * K + k, t.register, t.step * K)),
                                  start=k == 0, stop=False)
                    for k in range(K):
                        mm = pe.matmul(pR(t.mod(2)), ones_bf[:], cum[:, t.mod(2), k * E:(k + 1) * E],
                                       start=False, stop=k == K - 1)
                    mm.then_inc(b_R, 1)

            pipeline(pe, route, 4, 4)

            pe.wait_ge(b_cum, T)
            for k in range(K):
                mm = pe.matmul(count_ps, cum[:, T % 2, k * E:(k + 1) * E], ones_bf[:, 0:1],
                               start=k == 0, stop=k == K - 1)
            mm.then_inc(r_count, 1)
            pe.wait_ge(r_tiles, 1)
            pe.matmul(base_ps, tiles_bf[:], before[0:E, 0:E], start=True, stop=True).then_inc(r_base, 1)
            pe.matmul(end_ps, upto[0:E, 0:E], tiles_bf[:, 0:1], start=True, stop=True).then_inc(r_end, 1)
            pe.matmul(total_ps, ones_bf[0:E, 0:1], tiles_bf[:, 0:1], start=True, stop=True).then_inc(r_end, 1)
            pe.wait_ge(r_done, 1)
            pe.matmul(expert_ps, ones_bf[0:E, 0:1], done_bf[:], start=True, stop=True).then_inc(r_expert, 1)
            def place(n, u):
                after(pe, r_hot, n + 1, 2)
                first = n.register is None and n.offset == 0
                pe.matmul(slot_ps, lane_hot[:, u, :], tile_hot[:, u, :], start=first, stop=False,
                          skip_group_check=True).then_inc(r_used, 1)

            for u in range(HOT):
                place(At(u), u)
            with pe.Fori(1, T * K // HOT) as i:
                for u in range(HOT):
                    place(At(u, i, HOT), u)

            pe.wait_ge(weights_in, 16 * 2 * E // 8)
            pe.wait_ge(r_experts_ok, 2)
            pe.wait_ge(r_slot_ok, 2)

            def transpose_rows(t):
                after(pe, xg_in[t.mod(U)], t.div(U) + 1, 16)
                after(pe, e_Tc, t - 1)
                for c in range(C):
                    mm = pe.transpose(pT(t.mod(2))[:, c * P:(c + 1) * P], xg[:, t.mod(U), c * P:(c + 1) * P], ident[:])
                mm.then_inc(e_T, 1)

            def hidden(t, expert):
                after(pe, e_Tc, t + 1)
                after(pe, e_h, t - 1)
                for c in range(C):
                    mm = pe.matmul(pH(t.mod(2)), xgT[:, t.mod(2), c * P:(c + 1) * P],
                                   keys_sb[:, ds(expert * C + c, 1), :].rearrange("p a n -> p (a n)"),
                                   start=c == 0, stop=c == C - 1)
                mm.then_inc(e_H, 1)

            def transpose_hidden(t):
                after(pe, e_h, t + 1)
                after(pe, e_hT, t - 1)
                pe.transpose(pHT(t.mod(2)), hid[:, t.mod(2), :], ident[:]).then_inc(e_HT, 1)

            def result(t, expert):
                after(pe, e_hT, t + 1)
                after(pe, e_y, t - 1)
                pe.matmul(pO(t.mod(2)), hidT[:, t.mod(2), :],
                          values_sb[:, ds(expert, 1), :].rearrange("p a n -> p (a n)"),
                          start=True, stop=True).then_inc(e_Y, 1)

            def experts(at, n):
                return nc.values_load_multi_w_load_instructions(
                    expert_of[0:1, ds(at.value, n)], engines=[mybir.EngineType.PE], min_val=0, max_val=E - 1,
                    skip_runtime_bounds_check_because="they are clamped where they are made")[1]

            first = experts(At(0), 4)
            transpose_rows(At(0))
            transpose_rows(At(1))
            hidden(At(0), first[0])
            transpose_rows(At(2))
            hidden(At(1), first[1])
            transpose_hidden(At(0))

            def turn(t):
                ex = experts(t, 2 * U)
                for u in range(U):
                    transpose_rows(t + u + 3)
                    hidden(t + u + 2, ex[u + 2])
                    transpose_hidden(t + u + 1)
                    result(t + u, ex[u])

            all_turns(pe, turn)

        @block.scalar
        def _(act):
            act.dma_start(sel_sb[:], expert_sel).then_inc(sel_in, 16)
            act.dma_start(bq_rows[:], b_q.rearrange("(c p) -> c p", p=P)).then_inc(bq_in, 16)
            act.dma_start(gates_in[:, 0:1], g_xattn.rearrange("(a b) -> a b", a=1).broadcast_to([P, 1])).then_inc(g_in, 16)
            act.dma_start(gates_in[:, 1:2], g_ffn.rearrange("(a b) -> a b", a=1).broadcast_to([P, 1])).then_inc(g_in, 16)
            act.wait_ge(g_in, 32)
            act.activation(gate_tanh[:], gates_in[:], ACT.Tanh).then_inc(tanh_ok, 1)
            for n in range(B // 2):
                act.wait_ge(setup_t, n + 1)
                act.copy(ctxT[:, :, 2 * n * M:2 * (n + 1) * M].rearrange("p c (b m) -> p b c m", b=2),
                         bank[:, 2 + n, 0:2 * C * M].rearrange("p (b c m) -> p b c m", b=2, c=C)
                         ).then_inc(setup_t_copied, 1)
            act.wait_ge(setup_t, 5)
            act.copy(selT[:].rearrange("p c e -> p (c e)"), bank[:, 6, 0:C * E]).then_inc(setup_t_copied, 1)
            act.wait_ge(setup_t, 6)
            act.copy(bq_sb[:], bank[:, 7, 0:C]).then_inc(setup_t_copied, 1)
            for n in range(4):
                act.wait_ge(setup_m, n + 1)
                act.copy(m_sb[:, n * B // 2:(n + 1) * B // 2, :].rearrange("p b m -> p (b m)"),
                         bank[:, 2 + n, 0:HALF]).then_inc(setup_m_copied, 1)
            for half in range(2):
                act.wait_ge(setup_m, 5 + half)
                act.copy(bias_row[:, half * B // 2:(half + 1) * B // 2, :].rearrange("p b m -> p (b m)"),
                         bank[0:1, 6 + half, 0:HALF]).then_inc(setup_m_copied, 1)
            act.wait_ge(var_ok, 1)
            act.activation(std[:], var[:], ACT.Sqrt, bias=0.0).then_inc(std_ok, 1)

            def attend(at, s):
                if live(at, s, 0):
                    t = at
                    after(act, a_T, t + 1)
                    after(act, a_S, t - 1)
                    act.copy(xnT[:, t.mod(2), :], pT(t.mod(2))).then_inc(a_Tc, 1)
                if live(at, s, 1):
                    t = at - 1
                    after(act, a_max, t + 1)
                    after(act, a_PT, t - 1)
                    act.activation(probs[:, t.mod(2), :], pS(t.mod(2)), ACT.Exp, bias=neg_max[:, ds(t.value, 1)],
                                   accum_out=row_sum[:, ds(t.value, 1)]).then_inc(a_exp, 1)
                if live(at, s, 2):
                    t = at - 2
                    after(act, a_PT, t + 1)
                    after(act, a_O, t - 1)
                    act.copy(probsT[:, t.mod(2), :], pPT(t.mod(2))).then_inc(a_PTc, 1)

            pipeline(act, attend, 2, 2)
            act.wait_ge(var_ok, 2)
            act.activation(std[:], var[:], ACT.Sqrt, bias=0.0).then_inc(std_ok, 1)

            def route(at, s):
                if live(at, s, 0):
                    t = at
                    after(act, b_T, t + 1)
                    after(act, b_L, t - 1)
                    act.copy(xnT[:, t.mod(2), :], pT(t.mod(2))).then_inc(b_Tc, 1)
                if live(at, s, 1):
                    t = at - 1
                    after(act, b_L, t + 1)
                    after(act, b_at, t - 1)
                    act.activation(probs_sel[:, t.mod(2), :], pL(t.mod(2)), ACT.Sigmoid).then_inc(b_sel, 1)
                if live(at, s, 4):
                    t = at - 4
                    after(act, b_R, t + 1)
                    act.copy(row(rank, t), pR(t.mod(2))).then_inc(b_rank, 1)

            pipeline(act, route, 4, 4)
            act.wait_ge(weights_in, 16 * 2 * E // 8)
            act.dma_start(y_tiles[:, FULL * U:, :], values_sb[:, 0:NT - FULL * U, :]).then_inc(y_filled, 16)

            def rows_out(t):
                after(act, e_T, t + 1)
                after(act, e_H, t - 1)
                act.copy(xgT[:, t.mod(2), :], pT(t.mod(2))).then_inc(e_Tc, 1)

            for n in range(LEAD):
                rows_out(At(n))

            def turn(t):
                for u in range(U):
                    rows_out(t + u + 3)
                    after(act, e_Y, t + u + 1)
                    after(act, y_out[u], t.div(U), 16)
                    act.copy(y_sb[:, u, :], pO(u % 2)).then_inc(e_y, 1)

            all_turns(act, turn)

        @block.vector
        def _(dve):
            per = T // XCH

            def count_up(semaphore):
                counted = [0]

                def own(*instructions):
                    for ins in instructions:
                        ins.then_inc(semaphore, 1)
                    counted[0] += len(instructions)
                    dve.wait_ge(semaphore, counted[0])
                return own

            m_step = count_up(m_own)

            def mean_and_variance():
                even, odd = stats[:, :, 0, :], stats[:, :, 1, :]
                m_step(dve.tensor_tensor(moments[:, 0, :], even[:, :, 1], odd[:, :, 1], ALU.subtract),
                       dve.tensor_tensor(moments[:, 1, :], even[:, :, 2], odd[:, :, 2], ALU.add),
                       dve.tensor_tensor(moments[:, 2, :], even[:, :, 1], odd[:, :, 1], ALU.add))
                m_step(dve.tensor_tensor(moments[:, 3, :], moments[:, 0, :], moments[:, 0, :], ALU.mult),
                       dve.tensor_scalar(moments[:, 1, :], moments[:, 1, :], 1.0 / D, EPS, ALU.mult, ALU.add),
                       dve.tensor_scalar(mean[:], moments[:, 2, :], 0.5, None, ALU.mult))
                dve.scalar_tensor_tensor(out=var[:], in0=moments[:, 3, :], scalar=0.25, in1=moments[:, 1, :],
                                         op0=ALU.mult, op1=ALU.add).then_inc(var_ok, 1)

            for t in range(T):
                if t % per == 0:
                    dve.wait_ge(x_in[t // per], 16)
                dve.bn_stats(stats[:, t, :, :].rearrange("p a b -> p (a b)"), xs[:, t, :]).then_inc(a_stats, 1)
            dve.wait_ge(a_stats, T)
            mean_and_variance()
            dve.wait_ge(tanh_ok, 1)
            dve.wait_ge(setup_t, 4)
            dve.tensor_scalar(ctx_sb[:], ctx_sb[:], gate_tanh[0:M, 0:1], None, ALU.mult).then_inc(ctx_scaled, 1)
            dve.wait_ge(std_ok, 1)
            dve.reciprocal(rstd[:], std[:]).then_inc(rstd_ok, 1)
            dve.wait_ge(rstd_ok, 1)

            def attend(at, s):
                if live(at, s, 0):
                    t = at
                    after(dve, a_T, t - 1)
                    dve.tensor_scalar(xn[:, t.mod(2), :], row(xs, t), mean[:, ds(t.value, 1)],
                                      rstd[:, ds(t.value, 1)], ALU.subtract, ALU.mult).then_inc(a_xn, 1)
                if live(at, s, 2):
                    t = at - 2
                    after(dve, a_S, t + 1)
                    dve.tensor_reduce(neg_max[:, ds(t.value, 1)], pS(t.mod(2)), AX.X, ALU.max,
                                      negate=True).then_inc(a_max, 1)
                if live(at, s, 3):
                    t = at - 3
                    after(dve, a_exp, t + 1)
                    dve.reciprocal(inv_sum[:, ds(t.value, 1)], row_sum[:, ds(t.value, 1)]).then_inc(a_inv, 1)
                if live(at, s, 4):
                    t = at - 4
                    after(dve, a_O, t + 1)
                    after(dve, a_inv, t + 1)
                    dve.scalar_tensor_tensor(out=row(xs, t), in0=pO(t.mod(2)), scalar=inv_sum[:, ds(t.value, 1)],
                                             in1=row(xs, t), op0=ALU.mult, op1=ALU.add).then_inc(a_x2, 1)
                if live(at, s, 5):
                    t = at - 5
                    after(dve, a_x2, t + 1)
                    dve.bn_stats(stats[:, ds(t.value, 1), :, :].rearrange("p t a b -> p (t a b)"),
                                 row(xs, t)).then_inc(b_stats, 1)

            pipeline(dve, attend, 5, 2)
            dve.wait_ge(b_stats, T)
            dve.wait_ge(a_xn, T)
            mean_and_variance()
            dve.wait_ge(std_ok, 2)
            dve.reciprocal(rstd[:], std[:]).then_inc(rstd_ok, 1)
            dve.wait_ge(rstd_ok, 2)
            dve.wait_ge(a_T, T)
            dve.wait_ge(consts_ok, 8)

            def route(at, s):
                if live(at, s, 3):
                    after(dve, b_kept, at - 3 - 3)
                    after(dve, b_sel, at - 3 + 1)
                if live(at, s, 0):
                    t = at
                    after(dve, b_T, t - 3)
                    after(dve, xn_out[t.mod(4)], t.div(4), 16)
                    dve.tensor_scalar(xn[:, t.mod(4), :], row(xs, t), mean[:, ds(t.value, 1)],
                                      rstd[:, ds(t.value, 1)], ALU.subtract, ALU.mult).then_inc(b_xn, 1)
                if live(at, s, 3):
                    t = at - 3
                    dve.max(top[:, t.mod(4), :], probs_sel[:, t.mod(2), :]).then_inc(b_top, 1)
                    after(dve, b_top, t + 1)
                if live(at, s, 4):
                    t = at - 4
                    after(dve, b_at, t + 1)
                    dve.tensor_tensor(
                        chosen[:, ds(t.value * K, K), :],
                        iota_f[:, 0:E].rearrange("p (a e) -> p a e", a=1).broadcast_to([P, K, E]),
                        top_at[:, t.mod(4), 0:K].rearrange("p (k a) -> p k a", a=1).broadcast_to([P, K, E]),
                        ALU.is_equal).then_inc(b_hot, 1)
                if live(at, s, 3):
                    t = at - 3
                    dve.max_index(top_at[:, t.mod(4), :], top[:, t.mod(4), :],
                                  probs_sel[:, t.mod(2), :]).then_inc(b_at, 1)

            pipeline(dve, route, 4, 4)

            own = count_up(r_own)

            dve.wait_ge(r_count, 1)
            own(dve.tensor_scalar(count_i[:, 0:1], count_ps, float(P - 1), None, ALU.add))
            own(dve.tensor_scalar(count_i[:, 1:2], count_i[:, 0:1], P.bit_length() - 1, None,
                                  ALU.logical_shift_right))
            dve.tensor_copy(tiles_bf[:], count_i[:, 1:2].broadcast_to([E, P])).then_inc(r_tiles, 1)
            dve.wait_ge(r_end, 2)
            own(dve.tensor_scalar(base_sb[:], base_ps, float(P), None, ALU.mult))
            dve.tensor_copy(total_i[:], total_ps).then_inc(r_experts_ok, 1)
            own(dve.tensor_copy(end_f[:], end_ps))
            dve.tensor_scalar(done_bf[:], iota_f[0:E, :], end_f[:, 0:1], None, ALU.is_ge).then_inc(r_done, 1)

            dve.wait_ge(b_rank, T)
            own(dve.tensor_tensor(rank[:], rank[:],
                                  base_sb[:].rearrange("p (a e) -> p a e", a=1).broadcast_to([P, T, E]), ALU.add))
            for n in range(T // 4):
                own(dve.tensor_tensor(
                    picked.rearrange("p (t k) e -> p t k e", k=K),
                    chosen[:, n * 4 * K:(n + 1) * 4 * K, :].rearrange("p (t k) e -> p t k e", k=K),
                    rank[:, n * 4:(n + 1) * 4, :].rearrange("p t (a e) -> p t a e", a=1).broadcast_to([P, 4, K, E]),
                    ALU.mult))
                own(dve.tensor_reduce(pos_f[:, n * 4 * K:(n + 1) * 4 * K], picked, AX.X, ALU.add))
            dve.tensor_copy(pos_i[:], pos_f[:]).then_inc(r_pos_ok, 1)
            dve.wait_ge(r_pos_ok, 1)
            own(dve.tensor_scalar(part_i[:, 0, :], pos_i[:], P - 1, None, ALU.bitwise_and),
                dve.tensor_scalar(part_i[:, 1, :], pos_i[:], P.bit_length() - 1, None, ALU.logical_shift_right))
            own(dve.tensor_copy(lane_f[:], part_i[:, 0, :]),
                dve.tensor_copy(tile_f[:], part_i[:, 1, :]))

            def one_hots(n, u):
                after(dve, r_used, n - (HOT - 1))
                dve.tensor_scalar(lane_hot[:, u, :], iota_h[:], lane_f[:, ds(n.value, 1)], None,
                                  ALU.is_equal).then_inc(r_hot, 1)
                dve.tensor_scalar(tile_hot[:, u, :], iota_h[:], tile_f[:, ds(n.value, 1)],
                                  token_no[:, ds(n.div(K).value, 1)], ALU.is_equal, ALU.mult).then_inc(r_hot, 1)

            for u in range(HOT):
                one_hots(At(u), u)
            with dve.Fori(1, T * K // HOT) as i:
                for u in range(HOT):
                    one_hots(At(u, i, HOT), u)

            dve.wait_ge(r_expert, 1)
            own(dve.memset(expert_of[:], 0), dve.memset(slot_token[:], 1 << 20))
            dve.tensor_scalar(expert_of[:, 0:NT], expert_ps[:, 0:NT], float(E - 1), None,
                              ALU.min).then_inc(r_experts_ok, 1)
            dve.wait_ge(r_used, T * K)
            own(dve.tensor_scalar(empty_f[:], slot_ps, 0.0, float(2 * N), ALU.is_equal, ALU.mult))
            dve.scalar_tensor_tensor(out=slot_token[:, 0:NT], in0=slot_ps[:, 0:NT], scalar=-1.0,
                                     in1=empty_f[:, 0:NT], op0=ALU.add, op1=ALU.add).then_inc(r_slot_ok, 1)
            dve.wait_ge(b_kept, T)
            dve.tensor_scalar(gate[:], gate[:], gate_tanh[:, 1:2], None, ALU.mult).then_inc(r_slot_ok, 1)

            def relu(t):
                after(dve, e_H, t + 1)
                after(dve, e_HT, t - 1)
                dve.tensor_scalar(hid[:, t.mod(2), :], pH(t.mod(2)), 0.0, None, ALU.max).then_inc(e_h, 1)

            def hidden_out(t):
                after(dve, e_HT, t + 1)
                after(dve, e_Y, t - 1)
                dve.tensor_copy(hidT[:, t.mod(2), :], pHT(t.mod(2))).then_inc(e_hT, 1)

            relu(At(0))
            relu(At(1))
            hidden_out(At(0))

            def turn(t):
                for u in range(U):
                    relu(t + u + 2)
                    hidden_out(t + u + 1)

            all_turns(dve, turn)

            def combine(t):
                for k in range(K):
                    n = At(t.offset * K + k, t.register, t.step * K)
                    after(dve, yg_in[k], t + 1, 16)
                    after(dve, yg_used, n)
                    dve.scalar_tensor_tensor(out=row(xs, t), in0=yg[:, k, :], scalar=gate[:, ds(n.value, 1)],
                                             in1=row(xs, t), op0=ALU.mult, op1=ALU.add).then_inc(yg_used, 1)

            combine(At(0))
            with dve.Fori(1, T) as i:
                combine(At(0, i, 1))


_INS = ["x", "ctx_1024", "g_xattn", "g_ffn", "L0_xattn_W", "L0_xattn_b", "L0_ffn_expert_sel",
        "L0_ffn_keys", "L0_ffn_values"]


def kernel(**inputs):
    import numpy as np
    import concourse.bacc as bacc
    from concourse.bass_utils import run_bass_kernel_spmd

    nc = bacc.Bacc("TRN2", target_bir_lowering=False, num_devices=1)
    arrays, args = {}, []
    for name in _INS:
        a = np.ascontiguousarray(inputs[name])
        arrays[f"in_{name}"] = a
        args.append(nc.dram_tensor(f"in_{name}", a.shape, mybir.dt.from_np(a.dtype), kind="ExternalInput").ap())
    out = nc.dram_tensor("out", arrays["in_x"].shape, F32, kind="ExternalOutput").ap()
    flamingo_block(nc, *args, out)
    return run_bass_kernel_spmd(nc, [arrays], core_ids=[0]).results[0]["out"]
```
